# Optimizing a Trainium2 kernel written in Bass

```python
import numpy as np
import jax
import jax.numpy as jnp

def _softmax(x, axis=-1):
    return jax.nn.softmax(x, axis=axis)

def _gelu(x):
    return jax.nn.gelu(x, approximate=True)

def _silu(x):
    return jax.nn.silu(x)

def _sigmoid(x):
    return jax.nn.sigmoid(x)

def _layernorm(x, axis=-1, eps=1e-05):
    m = jnp.mean(x, axis=axis, keepdims=True)
    v = jnp.var(x, axis=axis, keepdims=True)
    return (x - m) / jnp.sqrt(v + eps)

def _scatter_add(tgt, idx, src, axis=0):
    return tgt.at[idx].add(src)

def _segment_sum(src, seg, n):
    return jax.ops.segment_sum(src, seg, n)
kernel_name = 'mk_dlrm_tower_d1_rec_r8_52d903'

def setup_inputs(seed: int=0):
    np.random.seed(seed)
    _w = jnp.asarray

    def _rec_inputs():
        import jax
        import jax.numpy as jnp
        _tk = jax.random.key(seed)
        ids = jnp.stack([jax.random.randint(jax.random.fold_in(_tk, 200 + f), (512,), 0, v, jnp.int32) for f, v in enumerate([12500, 12500, 1250, 12500, 12500, 125000, 1000, 1000, 1000, 12500, 12500, 1250, 1000, 1000, 12500, 1250, 12500, 12500, 1250, 1000, 1000, 1000, 1000, 1000, 1000, 1000])], axis=1)
        tbl_0 = 0.05 * jax.random.normal(jax.random.fold_in(_tk, 500 + 0), (12500, 128), jnp.float32)
        tbl_1 = 0.05 * jax.random.normal(jax.random.fold_in(_tk, 500 + 1), (12500, 128), jnp.float32)
        tbl_2 = 0.05 * jax.random.normal(jax.random.fold_in(_tk, 500 + 2), (1250, 128), jnp.float32)
        tbl_3 = 0.05 * jax.random.normal(jax.random.fold_in(_tk, 500 + 3), (12500, 128), jnp.float32)
        tbl_4 = 0.05 * jax.random.normal(jax.random.fold_in(_tk, 500 + 4), (12500, 128), jnp.float32)
        tbl_5 = 0.05 * jax.random.normal(jax.random.fold_in(_tk, 500 + 5), (125000, 128), jnp.float32)
        tbl_6 = 0.05 * jax.random.normal(jax.random.fold_in(_tk, 500 + 6), (1000, 128), jnp.float32)
        tbl_7 = 0.05 * jax.random.normal(jax.random.fold_in(_tk, 500 + 7), (1000, 128), jnp.float32)
        tbl_8 = 0.05 * jax.random.normal(jax.random.fold_in(_tk, 500 + 8), (1000, 128), jnp.float32)
        tbl_9 = 0.05 * jax.random.normal(jax.random.fold_in(_tk, 500 + 9), (12500, 128), jnp.float32)
        tbl_10 = 0.05 * jax.random.normal(jax.random.fold_in(_tk, 500 + 10), (12500, 128), jnp.float32)
        tbl_11 = 0.05 * jax.random.normal(jax.random.fold_in(_tk, 500 + 11), (1250, 128), jnp.float32)
        tbl_12 = 0.05 * jax.random.normal(jax.random.fold_in(_tk, 500 + 12), (1000, 128), jnp.float32)
        tbl_13 = 0.05 * jax.random.normal(jax.random.fold_in(_tk, 500 + 13), (1000, 128), jnp.float32)
        tbl_14 = 0.05 * jax.random.normal(jax.random.fold_in(_tk, 500 + 14), (12500, 128), jnp.float32)
        tbl_15 = 0.05 * jax.random.normal(jax.random.fold_in(_tk, 500 + 15), (1250, 128), jnp.float32)
        tbl_16 = 0.05 * jax.random.normal(jax.random.fold_in(_tk, 500 + 16), (12500, 128), jnp.float32)
        tbl_17 = 0.05 * jax.random.normal(jax.random.fold_in(_tk, 500 + 17), (12500, 128), jnp.float32)
        tbl_18 = 0.05 * jax.random.normal(jax.random.fold_in(_tk, 500 + 18), (1250, 128), jnp.float32)
        tbl_19 = 0.05 * jax.random.normal(jax.random.fold_in(_tk, 500 + 19), (1000, 128), jnp.float32)
        tbl_20 = 0.05 * jax.random.normal(jax.random.fold_in(_tk, 500 + 20), (1000, 128), jnp.float32)
        tbl_21 = 0.05 * jax.random.normal(jax.random.fold_in(_tk, 500 + 21), (1000, 128), jnp.float32)
        tbl_22 = 0.05 * jax.random.normal(jax.random.fold_in(_tk, 500 + 22), (1000, 128), jnp.float32)
        tbl_23 = 0.05 * jax.random.normal(jax.random.fold_in(_tk, 500 + 23), (1000, 128), jnp.float32)
        tbl_24 = 0.05 * jax.random.normal(jax.random.fold_in(_tk, 500 + 24), (1000, 128), jnp.float32)
        tbl_25 = 0.05 * jax.random.normal(jax.random.fold_in(_tk, 500 + 25), (1000, 128), jnp.float32)
        _rk = jax.random.fold_in(_tk, 7)
        r_dense_features = -0.000292821 + 1.00034 * jax.random.normal(jax.random.fold_in(_rk, 101), (512, 128), jnp.float32)
        W_top1 = 0.0405887 * jax.random.normal(jax.random.fold_in(_tk, 801), (607, 512), jnp.float32)
        W_top2 = 0.0441942 * jax.random.normal(jax.random.fold_in(_tk, 802), (512, 256), jnp.float32)
        W_top3 = 0.0625 * jax.random.normal(jax.random.fold_in(_tk, 803), (256, 1), jnp.float32)
        b_top1 = jnp.zeros((512,), jnp.float32)
        b_top2 = jnp.zeros((256,), jnp.float32)
        return (r_dense_features, ids, tbl_0, tbl_1, tbl_2, tbl_3, tbl_4, tbl_5, tbl_6, tbl_7, tbl_8, tbl_9, tbl_10, tbl_11, tbl_12, tbl_13, tbl_14, tbl_15, tbl_16, tbl_17, tbl_18, tbl_19, tbl_20, tbl_21, tbl_22, tbl_23, tbl_24, tbl_25, W_top1, b_top1, W_top2, b_top2, W_top3)
    r_dense_features, ids, tbl_0, tbl_1, tbl_2, tbl_3, tbl_4, tbl_5, tbl_6, tbl_7, tbl_8, tbl_9, tbl_10, tbl_11, tbl_12, tbl_13, tbl_14, tbl_15, tbl_16, tbl_17, tbl_18, tbl_19, tbl_20, tbl_21, tbl_22, tbl_23, tbl_24, tbl_25, W_top1, b_top1, W_top2, b_top2, W_top3 = _rec_inputs()

    def _L0_rec_setup():
        import jax, jax.numpy as jnp
        import numpy as np
        F = 26
        _TRIU_I, _TRIU_J = np.triu_indices(F + 1, k=1)
        key = jax.random.key(seed)
        k1, k2 = jax.random.split(key)
        B, D = (4096, 128)
        dense_features = jax.random.normal(k1, (B, D), dtype=jnp.float32)
        sparse_features = jax.random.normal(k2, (B, F, D), dtype=jnp.float32)
        return {'dense_features': dense_features, 'sparse_features': sparse_features}
    _L0_rec_all = _L0_rec_setup()
    _L0_rec_in = {k: v for k, v in _L0_rec_all.items() if k in ()}
    del _L0_rec_all
    return {'r_dense_features': r_dense_features, 'ids': ids, 'tbl_0': tbl_0, 'tbl_1': tbl_1, 'tbl_2': tbl_2, 'tbl_3': tbl_3, 'tbl_4': tbl_4, 'tbl_5': tbl_5, 'tbl_6': tbl_6, 'tbl_7': tbl_7, 'tbl_8': tbl_8, 'tbl_9': tbl_9, 'tbl_10': tbl_10, 'tbl_11': tbl_11, 'tbl_12': tbl_12, 'tbl_13': tbl_13, 'tbl_14': tbl_14, 'tbl_15': tbl_15, 'tbl_16': tbl_16, 'tbl_17': tbl_17, 'tbl_18': tbl_18, 'tbl_19': tbl_19, 'tbl_20': tbl_20, 'tbl_21': tbl_21, 'tbl_22': tbl_22, 'tbl_23': tbl_23, 'tbl_24': tbl_24, 'tbl_25': tbl_25, 'W_top1': W_top1, 'b_top1': b_top1, 'W_top2': W_top2, 'b_top2': b_top2, 'W_top3': W_top3}

def reference(r_dense_features, ids, tbl_0, tbl_1, tbl_2, tbl_3, tbl_4, tbl_5, tbl_6, tbl_7, tbl_8, tbl_9, tbl_10, tbl_11, tbl_12, tbl_13, tbl_14, tbl_15, tbl_16, tbl_17, tbl_18, tbl_19, tbl_20, tbl_21, tbl_22, tbl_23, tbl_24, tbl_25, W_top1, b_top1, W_top2, b_top2, W_top3):
    import jax
    import jax.numpy as jnp

    def _L0_rec_ref(dense_features, sparse_features):
        import jax, jax.numpy as jnp
        import numpy as np
        F = 26
        _TRIU_I, _TRIU_J = np.triu_indices(F + 1, k=1)
        combined = jnp.concatenate([dense_features[:, None, :], sparse_features], axis=1)
        interactions = jnp.einsum('bfd,bgd->bfg', combined, combined)
        interactions_flat = interactions[:, _TRIU_I, _TRIU_J]
        return jnp.concatenate([dense_features, interactions_flat], axis=1)
    e = jnp.stack([tbl_0[ids[:, 0]], tbl_1[ids[:, 1]], tbl_2[ids[:, 2]], tbl_3[ids[:, 3]], tbl_4[ids[:, 4]], tbl_5[ids[:, 5]], tbl_6[ids[:, 6]], tbl_7[ids[:, 7]], tbl_8[ids[:, 8]], tbl_9[ids[:, 9]], tbl_10[ids[:, 10]], tbl_11[ids[:, 11]], tbl_12[ids[:, 12]], tbl_13[ids[:, 13]], tbl_14[ids[:, 14]], tbl_15[ids[:, 15]], tbl_16[ids[:, 16]], tbl_17[ids[:, 17]], tbl_18[ids[:, 18]], tbl_19[ids[:, 19]], tbl_20[ids[:, 20]], tbl_21[ids[:, 21]], tbl_22[ids[:, 22]], tbl_23[ids[:, 23]], tbl_24[ids[:, 24]], tbl_25[ids[:, 25]]], axis=1)
    z = _L0_rec_ref(r_dense_features, e)
    z = z.reshape(z.shape[0], -1)
    h = jnp.concatenate([z, r_dense_features], axis=1)
    h = jnp.maximum(h @ W_top1 + b_top1, 0.0)
    h = jnp.maximum(h @ W_top2 + b_top2, 0.0)
    y = h @ W_top3
    return y

_drawn_inputs = setup_inputs


def setup_inputs(seed=0):
    import zlib

    import numpy as np

    out = dict(_drawn_inputs(seed))
    spreads = {'b_top1': (0.0, 0.1), 'b_top2': (0.0, 0.1)}
    factors = {}
    for name, (base, spread) in spreads.items():
        noise = np.random.default_rng([zlib.crc32(name.encode()), seed]).standard_normal(out[name].shape)
        drawn = base * np.exp(spread * noise) if base else spread * noise
        out[name] = jnp.asarray(drawn.astype(out[name].dtype))
    for name, factor in factors.items():
        out[name] = (out[name] * factor).astype(out[name].dtype)
    return out
```

```python
import concourse.bass as bass
from concourse import mybir
from contextlib import ExitStack

P = 128
NF = 26
D = 128
BATCH = 512
TILES = BATCH // P
SLOTS = NF + 1
ROWS = 32
QUADS = 4
HALF = (SLOTS - 1) // 2
Z_CHUNKS = 3
Z_RUNS = SLOTS // Z_CHUNKS
Z_ROWS = Z_RUNS * HALF
WRAP = SLOTS + HALF
H1, H2 = 512, 256
M1, M2 = H1 // P, H2 // P

OH_TABLES = 5
G_TABLES = NF - OH_TABLES
OH_ROUNDS = [3, OH_TABLES - 3]
DENSE_SLOT = G_TABLES
OH_SLOT = G_TABLES + 1
VOCAB = 1000
CH = 8
VP = VOCAB // CH


def groups_of(n, count):
    cuts = [n * i // count for i in range(count + 1)]
    return list(zip(cuts[:-1], cuts[1:]))


GROUPS = groups_of(1 + G_TABLES, 6)
NG = len(GROUPS)


def dlrm_tower(nc, dense, ids_p, ids_t, tables, w1_pairs, w1_dense, b1, w2, b2, w3, out):
    f32, i32, u32 = mybir.dt.float32, mybir.dt.int32, mybir.dt.uint32
    ALU, ACT = mybir.AluOpType, mybir.ActivationFunctionType

    with ExitStack() as ctx:
        def sb(name, shape, dt=f32):
            return ctx.enter_context(nc.sbuf_tensor(name, shape, dt))

        def bank(name, cols=512):
            return ctx.enter_context(nc.psum_tensor(name, [P, cols], f32))

        def sem(name):
            return ctx.enter_context(nc.semaphore(name))

        ident = sb("ident", [P, P])
        row_id = sb("row_id", [P, CH])
        ids_sb = sb("ids_sb", [P, TILES, NF], i32)
        ids_bc = sb("ids_bc", [P, OH_TABLES, P], i32)
        tab_sb = sb("tab_sb", [P, OH_TABLES, CH, D])
        onehot = [sb(f"onehot{r}", [P, n, CH, P]) for r, n in enumerate(OH_ROUNDS)]
        emb = sb("emb", [P, 1 + G_TABLES, D])
        XT = sb("XT", [P, P, ROWS])
        denseT = sb("denseT", [P, P])
        Zd = sb("Zd", [P, ROWS * (WRAP + 1)])
        pairs = sb("pairs", [P, SLOTS * HALF])
        zT = sb("zT", [P, Z_CHUNKS, P])
        w1_sb = sb("w1_sb", [P, Z_CHUNKS, H1])
        w1d_sb = sb("w1d_sb", [P, 2, H1])
        w1s_sb = sb("w1s_sb", [P, H1])
        w2_sb = sb("w2_sb", [P, M1, H2])
        w3_sb = sb("w3_sb", [P, M2])
        b1_sb = sb("b1_sb", [P, M1])
        b2_sb = sb("b2_sb", [P, M2])
        h1T = sb("h1T", [P, M1, P])
        h2T = sb("h2T", [P, M2, P])
        y_row = sb("y_row", [1, BATCH])

        bank_xt = [bank("bank_xt0"), bank("bank_xt1")]
        bank_gram = bank("bank_gram", 1024)
        bank_z = bank("bank_z")
        bank_h2 = bank("bank_h2")
        bank_oh = bank("bank_oh")
        bank_ids = bank("bank_ids")

        ids_loaded = sem("ids_loaded")
        ids_bc_loaded = sem("ids_bc_loaded")
        tab_loaded = [sem(f"tab_loaded{r}") for r in range(len(OH_ROUNDS))]
        w1d_loaded = sem("w1d_loaded")
        weights_loaded = sem("weights_loaded")
        dense_loaded = sem("dense_loaded")
        gathered = [sem(f"gathered{g}") for g in range(NG)]
        consts_part = sem("consts_part")
        consts_ready = sem("consts_ready")
        pad_zeroed = sem("pad_zeroed")
        w1s_ready = sem("w1s_ready")
        transposed = sem("transposed")
        xt_ready = [sem("xt_ready0"), sem("xt_ready1")]
        ids_spread = sem("ids_spread")
        onehot_ready = sem("onehot_ready")
        picked = sem("picked")
        picked_laid = sem("picked_laid")
        gram_ready = sem("gram_ready")
        gram_spread = sem("gram_spread")
        pairs_ready = sem("pairs_ready")
        z_ready = sem("z_ready")
        zT_ready = sem("zT_ready")
        h1_sum = sem("h1_sum")
        h1_act = sem("h1_act")
        h1_dve = sem("h1_dve")
        h2_sum = sem("h2_sum")
        h2_act = sem("h2_act")
        h2_dve = sem("h2_dve")
        y_sum = sem("y_sum")
        y_ready = sem("y_ready")
        stored = sem("stored")

        R = len(OH_ROUNDS)
        oh_first = [sum(OH_ROUNDS[:r]) for r in range(R)]
        g_dmas = [min(hi, G_TABLES) - lo for lo, hi in GROUPS]

        block = ctx.enter_context(nc.Block())

        @block.sync
        def _(sp):
            def load_dense(t):
                sp.dma_start(emb[:, DENSE_SLOT, :], dense[bass.ds(t * P, P), :]).then_inc(dense_loaded, 16)

            def load_ids_bc(t):
                src = ids_t[bass.ds(t, 1), G_TABLES:NF, :].rearrange("a f b -> a (f b)").to_broadcast((VP, OH_TABLES * P))
                sp.dma_start(ids_bc[0:VP, :, :].rearrange("p f b -> p (f b)"), src).then_inc(ids_bc_loaded, 16)

            sp.dma_start(ids_sb[:, :, :], ids_p).then_inc(ids_loaded, 16)
            load_ids_bc(0)
            load_dense(0)
            for r, n in enumerate(OH_ROUNDS):
                for k in range(oh_first[r], oh_first[r] + n):
                    sp.dma_start(tab_sb[0:VP, k, :, :],
                                 tables[G_TABLES + k].rearrange("(p c) d -> p c d", c=CH)).then_inc(tab_loaded[r], 16)
            sp.dma_start(w1d_sb[:, :, :], w1_dense.rearrange("(a p) h -> p a h", p=P)).then_inc(w1d_loaded, 16)
            sp.dma_start(w1_sb[0:Z_ROWS, :, :], w1_pairs.rearrange("(q k) h -> k q h", k=Z_ROWS)).then_inc(weights_loaded, 16)
            sp.dma_start(w2_sb[:, :, :], w2.rearrange("(k p) h -> p k h", p=P)).then_inc(weights_loaded, 16)
            sp.dma_start(b1_sb[:, :], b1).then_inc(weights_loaded, 16)
            sp.dma_start(b2_sb[:, :], b2).then_inc(weights_loaded, 16)
            sp.dma_start(w3_sb[:, :], w3).then_inc(weights_loaded, 16)

            with sp.Fori(0, TILES - 1) as t:
                sp.wait_ge(ids_spread, t * R + R)
                load_ids_bc(t + 1)
                sp.wait_ge(transposed, t * NG + NG)
                load_dense(t + 1)
            sp.wait_ge(y_ready, TILES)
            sp.dma_start(out.rearrange("b o -> o b"), y_row[:, :]).then_inc(stored, 16)
            sp.wait_ge(stored, 16)

        @block.gpsimd
        def _(pool):
            pool.memset(ident[:, :], 0.0).then_inc(consts_part, 1)
            pool.iota(row_id[:, :], pattern=[[1, CH]], base=0, channel_multiplier=CH,
                      allow_small_or_imprecise_dtypes=True).then_inc(consts_ready, 1)
            pool.wait_ge(consts_part, 1)
            pool.affine_select(out=ident[:, :], in_=ident[:, :], compare_op=ALU.not_equal, fill=1.0,
                               base=0, pattern=[[-1, P]], channel_multiplier=1).then_inc(consts_ready, 1)

            def gather_group(t, g):
                lo, hi = GROUPS[g]
                for f in range(lo, min(hi, G_TABLES)):
                    pool.indirect_dma_start(
                        out=emb[:, f, :], out_offset=None, in_=tables[f][:, :],
                        in_offset=bass.IndirectOffsetOnAxis(ap=ids_sb[:, t, f:f + 1].bitcast(u32), axis=0),
                    ).then_inc(gathered[g], 16)

            pool.wait_ge(ids_loaded, 16)
            for t in range(TILES):
                for g in range(NG):
                    if t:
                        pool.wait_ge(transposed, (t - 1) * NG + g + 1)
                    gather_group(t, g)

        @block.tensor
        def _(pe):
            def pick_rows(t, r):
                pe.wait_ge(onehot_ready, t * R + r + 1)
                pe.wait_ge(picked_laid, t * R + r)
                for j in range(OH_ROUNDS[r]):
                    for c in range(CH):
                        last = nc.tensor.matmul(bank_oh[:, j * P:(j + 1) * P],
                                                tab_sb[0:VP, oh_first[r] + j, c, :],
                                                onehot[r][0:VP, j, c, :],
                                                start=(c == 0), stop=(c == CH - 1))
                last.then_inc(picked, 1)

            def transpose_group(t, g):
                lo, hi = GROUPS[g]
                pe.wait_ge(gathered[g], t * (16 * g_dmas[g]) + 16 * g_dmas[g])
                if g == NG - 1:
                    pe.wait_ge(dense_loaded, t * 16 + 16)
                pe.wait_ge(xt_ready[g % 2], t * (NG // 2) + g // 2)
                for slot in range(lo, hi):
                    last = nc.tensor.transpose(bank_xt[g % 2][:, (slot - lo) * P:(slot - lo + 1) * P],
                                               emb[:, slot, :], ident[:, :])
                last.then_inc(transposed, 1)

            def tile(t, more):
                pe.wait_ge(xt_ready[0], t * (NG // 2) + NG // 2)
                pe.wait_ge(xt_ready[1], t * (NG // 2) + NG // 2)
                pe.wait_ge(picked_laid, t * R + R)
                pe.wait_ge(h1_act, t)
                pe.wait_ge(h1_dve, t)
                for i in range(P // QUADS):
                    for s in range(QUADS):
                        b = s * ROWS + i
                        last = nc.tensor.matmul(bank_gram[s * ROWS:(s + 1) * ROWS, i * ROWS:i * ROWS + SLOTS],
                                                XT[:, b, :], XT[:, b, 0:SLOTS], start=True, stop=True)
                last.then_inc(gram_ready, 1)
                if more:
                    transpose_group(t + 1, 0)
                    transpose_group(t + 1, 1)
                    pick_rows(t + 1, 0)
                    transpose_group(t + 1, 2)
                    pick_rows(t + 1, 1)
                    transpose_group(t + 1, 3)
                pe.wait_ge(pairs_ready, t + 1)
                pe.wait_ge(h2_act, t)
                for q in range(Z_CHUNKS):
                    last = nc.tensor.transpose(bank_z[0:Z_ROWS, q * P:(q + 1) * P],
                                               pairs[:, q * Z_ROWS:(q + 1) * Z_ROWS], ident[:, :])
                last.then_inc(z_ready, 1)
                pe.wait_ge(zT_ready, t + 1)
                pe.wait_ge(w1s_ready, 1)
                pe.wait_ge(weights_loaded, 16 * 5)
                for m in range(M1):
                    sums = bank_gram[:, (m // 2) * 512 + (m % 2) * P:(m // 2) * 512 + (m % 2 + 1) * P]
                    cols = slice(m * P, (m + 1) * P)
                    nc.tensor.matmul(sums, w1s_sb[:, cols], denseT[:, :], start=True, stop=False)
                    for q in range(Z_CHUNKS):
                        last = nc.tensor.matmul(sums, w1_sb[0:Z_ROWS, q, cols], zT[0:Z_ROWS, q, :],
                                                start=False, stop=(q == Z_CHUNKS - 1))
                    if m % 2:
                        last.then_inc(h1_sum, 1)
                if more:
                    transpose_group(t + 1, 4)
                pe.wait_ge(h1_act, t + 1)
                pe.wait_ge(h2_dve, t)
                pe.wait_ge(y_ready, t)
                for m in range(M2):
                    sums = (bank_z, bank_h2)[m][:, 0:P]
                    for k in range(M1):
                        if m == 0 and k == M1 // 2:
                            pe.wait_ge(h1_dve, t + 1)
                        last = nc.tensor.matmul(sums, w2_sb[:, k, m * P:(m + 1) * P], h1T[:, k, :],
                                                start=(k == 0), stop=(k == M1 - 1))
                    last.then_inc(h2_sum, 1)
                if more:
                    transpose_group(t + 1, 5)
                pe.wait_ge(h2_act, t + 1)
                pe.wait_ge(h2_dve, t + 1)
                for k in range(M2):
                    last = nc.tensor.matmul(bank_h2[0:1, 2 * P:3 * P], w3_sb[:, k:k + 1], h2T[:, k, :],
                                            start=(k == 0), stop=(k == M2 - 1))
                last.then_inc(y_sum, 1)

            for r in range(R):
                pe.wait_ge(tab_loaded[r], 16 * OH_ROUNDS[r])
                pick_rows(0, r)
            pe.wait_ge(consts_ready, 2)
            for g in range(NG):
                transpose_group(0, g)
            tile(0, True)
            with pe.Fori(1, TILES - 1) as t:
                tile(t, True)
            tile(TILES - 1, False)

        @block.vector
        def _(dve):
            def compare(t, r):
                n = OH_ROUNDS[r]
                dve.wait_ge(ids_spread, t * R + r + 1)
                for j in range(n):
                    last = nc.vector.tensor_tensor(
                        onehot[r][0:VP, j, :, :],
                        bank_ids[0:VP, j * P:(j + 1) * P].rearrange("p (a b) -> p a b", a=1).to_broadcast((VP, CH, P)),
                        row_id[0:VP, :].rearrange("p (c a) -> p c a", a=1).to_broadcast((VP, CH, P)),
                        ALU.is_equal)
                last.then_inc(onehot_ready, 1)

            def lay_group(t, g):
                lo, hi = GROUPS[g]
                dve.wait_ge(transposed, t * NG + g + 1)
                nc.vector.tensor_copy(XT[:, :, lo:hi].rearrange("p b s -> p s b"),
                                      bank_xt[0][:, 0:(hi - lo) * P].rearrange("p (s b) -> p s b", b=P)
                                      ).then_inc(xt_ready[0], 1)

            def tile(t, more):
                if more:
                    for r in range(R):
                        dve.wait_ge(picked, t * R + r + 1)
                        compare(t + 1, r)
                dve.wait_ge(gram_ready, t + 1)
                dve.wait_ge(pairs_ready, t)
                gram = bank_gram[:, :].rearrange("p (i c) -> p c i", c=ROWS)
                zd = Zd[:, 0:ROWS * WRAP].rearrange("p (r c) -> p c r", c=WRAP)
                nc.vector.transpose(zd[:, 0:SLOTS, :], gram[:, 0:SLOTS, :])
                nc.vector.transpose(zd[:, SLOTS:WRAP, :], gram[:, 0:HALF, :]).then_inc(gram_spread, 1)
                if more:
                    lay_group(t + 1, 0)
                    lay_group(t + 1, 2)
                dve.wait_ge(h1_sum, t * 2 + 2)
                for m in range(M1 // 2, M1):
                    last = nc.vector.tensor_scalar(h1T[:, m, :], bank_gram[:, 512 + (m % 2) * P:512 + (m % 2 + 1) * P],
                                                   b1_sb[:, m:m + 1], 0.0, ALU.add, ALU.max)
                last.then_inc(h1_dve, 1)
                if more:
                    lay_group(t + 1, 4)
                dve.wait_ge(h2_sum, t * 2 + 2)
                nc.vector.tensor_scalar(h2T[:, 1, :], bank_h2[:, 0:P], b2_sb[:, 1:2], 0.0,
                                        ALU.add, ALU.max).then_inc(h2_dve, 1)

            nc.vector.memset(XT[:, :, SLOTS:ROWS], 0.0).then_inc(pad_zeroed, 1)
            dve.wait_ge(consts_ready, 2)
            for r in range(R):
                compare(0, r)
            dve.wait_ge(w1d_loaded, 16)
            nc.vector.tensor_tensor(w1s_sb[:, :], w1d_sb[:, 0, :], w1d_sb[:, 1, :], ALU.add).then_inc(w1s_ready, 1)
            dve.wait_ge(weights_loaded, 16 * 5)
            for g in range(0, NG, 2):
                lay_group(0, g)
            tile(0, True)
            with dve.Fori(1, TILES - 1) as t:
                tile(t, True)
            tile(TILES - 1, False)

        @block.scalar
        def _(act):
            def spread_ids(t, r):
                a, n = oh_first[r], OH_ROUNDS[r]
                if r == 0:
                    act.wait_ge(ids_bc_loaded, t * 16 + 16)
                act.wait_ge(onehot_ready, t * R + r)
                nc.scalar.copy(bank_ids[0:VP, 0:n * P],
                               ids_bc[0:VP, a:a + n, :].rearrange("p f b -> p (f b)")).then_inc(ids_spread, 1)

            def lay_picked(t, r):
                a, n = oh_first[r], OH_ROUNDS[r]
                act.wait_ge(picked, t * R + r + 1)
                slot = OH_SLOT + a
                nc.scalar.copy(XT[:, :, slot:slot + n].rearrange("p b s -> p s b"),
                               bank_oh[:, 0:n * P].rearrange("p (s b) -> p s b", b=P)).then_inc(picked_laid, 1)

            def lay_group(t, g):
                lo, hi = GROUPS[g]
                act.wait_ge(transposed, t * NG + g + 1)
                if g == NG - 1:
                    nc.scalar.copy(denseT[:, :], bank_xt[1][:, (DENSE_SLOT - lo) * P:(DENSE_SLOT - lo + 1) * P])
                nc.scalar.copy(XT[:, :, lo:hi].rearrange("p b s -> p s b"),
                               bank_xt[1][:, 0:(hi - lo) * P].rearrange("p (s b) -> p s b", b=P)
                               ).then_inc(xt_ready[1], 1)

            def tile(t, more):
                if more:
                    for r in range(R):
                        spread_ids(t + 1, r)
                act.wait_ge(gram_spread, t + 1)
                act.wait_ge(z_ready, t)
                nc.scalar.copy(pairs[:, :].rearrange("p (j s) -> p j s", s=HALF),
                               Zd[:, :].rearrange("p (r c) -> p r c", c=WRAP + 1)[:, 0:SLOTS, 1:1 + HALF]
                               ).then_inc(pairs_ready, 1)
                if more:
                    lay_group(t + 1, 1)
                    lay_picked(t + 1, 0)
                    lay_picked(t + 1, 1)
                    lay_group(t + 1, 3)
                act.wait_ge(z_ready, t + 1)
                nc.scalar.copy(zT[0:Z_ROWS, :, :].rearrange("p q b -> p (q b)"),
                               bank_z[0:Z_ROWS, 0:Z_CHUNKS * P]).then_inc(zT_ready, 1)
                act.wait_ge(h1_sum, t * 2 + 1)
                for m in range(M1 // 2):
                    last = nc.scalar.activation(h1T[:, m, :], bank_gram[:, m * P:(m + 1) * P], ACT.Relu,
                                                bias=b1_sb[:, m:m + 1])
                last.then_inc(h1_act, 1)
                act.wait_ge(h2_sum, t * 2 + 1)
                nc.scalar.activation(h2T[:, 0, :], bank_z[:, 0:P], ACT.Relu, bias=b2_sb[:, 0:1]).then_inc(h2_act, 1)
                if more:
                    lay_group(t + 1, 5)
                act.wait_ge(y_sum, t + 1)
                nc.scalar.copy(y_row[:, bass.ds(t * P, P)], bank_h2[0:1, 2 * P:3 * P]).then_inc(y_ready, 1)

            for r in range(R):
                spread_ids(0, r)
            act.wait_ge(pad_zeroed, 1)
            for r in range(R):
                lay_picked(0, r)
            for g in range(1, NG, 2):
                lay_group(0, g)
            act.wait_ge(weights_loaded, 16 * 5)
            tile(0, True)
            with act.Fori(1, TILES - 1) as t:
                tile(t, True)
            tile(TILES - 1, False)


def pair_rows():
    feature = list(range(1, 1 + G_TABLES)) + [0] + list(range(1 + G_TABLES, SLOTS))
    order = []
    for j in range(SLOTS):
        for step in range(1, HALF + 1):
            a, b = sorted((feature[j], feature[(j + step) % SLOTS]))
            order.append(D + a * (2 * SLOTS - a - 1) // 2 + (b - a - 1))
    return order


def kernel(**inputs):
    import numpy as np
    import concourse.bacc as bacc
    from concourse import mybir as mb
    from concourse.bass_utils import run_bass_kernel_spmd

    ids = np.asarray(inputs["ids"])
    w1 = np.asarray(inputs["W_top1"])
    n_pairs = SLOTS * HALF
    laid = {
        "dense": np.asarray(inputs["r_dense_features"]),
        "ids_p": ids.reshape(TILES, P, NF).transpose(1, 0, 2),
        "ids_t": ids.reshape(TILES, P, NF).transpose(0, 2, 1),
        "w1_pairs": w1[np.array(pair_rows())],
        "w1_dense": np.concatenate([w1[0:D], w1[D + n_pairs:]]),
        "b1": np.asarray(inputs["b_top1"]).reshape(M1, P).transpose(),
        "w2": np.asarray(inputs["W_top2"]),
        "b2": np.asarray(inputs["b_top2"]).reshape(M2, P).transpose(),
        "w3": np.asarray(inputs["W_top3"]).reshape(M2, P).transpose(),
    }
    for f in range(NF):
        laid[f"tbl_{f}"] = np.asarray(inputs[f"tbl_{f}"])

    nc = bacc.Bacc("TRN2", target_bir_lowering=False, num_devices=1)
    arrays, args = {}, {}
    for name, a in laid.items():
        a = np.ascontiguousarray(a)
        arrays[f"in_{name}"] = a
        args[name] = nc.dram_tensor(f"in_{name}", a.shape, mb.dt.from_np(a.dtype), kind="ExternalInput").ap()
    out = nc.dram_tensor("out_y", (BATCH, 1), mb.dt.float32, kind="ExternalOutput").ap()
    tables = [args.pop(f"tbl_{f}") for f in range(NF)]
    dlrm_tower(nc, tables=tables, out=out, **args)
    result = run_bass_kernel_spmd(nc, [arrays], core_ids=[0])
    return result.results[0]["out_y"]
```

```python
import concourse.bass as bass
from concourse import mybir
from contextlib import ExitStack

P = 128
NF = 26
D = 128
BATCH = 512
TILES = BATCH // P
SLOTS = NF + 1
ROWS = 32
QUADS = 4
HALF = (SLOTS - 1) // 2
Z_CHUNKS = 3
Z_RUNS = SLOTS // Z_CHUNKS
Z_ROWS = Z_RUNS * HALF
WRAP = SLOTS + HALF
H1, H2 = 512, 256
M1, M2 = H1 // P, H2 // P

OH_TABLES = 6
G_TABLES = NF - OH_TABLES
DENSE_SLOT = G_TABLES
OH_SLOT = G_TABLES + 1
VOCAB = 1000
CH = 8
VP = VOCAB // CH
ACT_COMPARES = (1, 4)
DVE_COMPARES = (0, 2, 3, 5)
OH_BUFFERS = 3

GROUPS = [(0, 4), (4, 8), (8, 12), (12, 16), (16, 19), (19, 21)]
NG = len(GROUPS)
assert GROUPS[-1][1] == OH_SLOT


def dlrm_tower(nc, dense, ids_p, ids_t, tables, w1_pairs, w1_dense, b1, w2, b2, w3, out):
    f32, bf16, i32, u32 = mybir.dt.float32, mybir.dt.bfloat16, mybir.dt.int32, mybir.dt.uint32
    ALU, ACT = mybir.AluOpType, mybir.ActivationFunctionType

    with ExitStack() as ctx:
        def sb(name, shape, dt=f32):
            return ctx.enter_context(nc.sbuf_tensor(name, shape, dt))

        def bank(name, cols=512):
            return ctx.enter_context(nc.psum_tensor(name, [P, cols], f32))

        def sem(name):
            return ctx.enter_context(nc.semaphore(name))

        def sems(name, n):
            return [sem(f"{name}{i}") for i in range(n)]

        ident = sb("ident", [P, P])
        row_id = sb("row_id", [P, CH])
        neg_row_id = sb("neg_row_id", [P, CH])
        ids_sb = sb("ids_sb", [P, TILES, NF], i32)
        ids_bc = sb("ids_bc", [P, OH_TABLES, BATCH], i32)
        tab = sb("tab", [P, OH_TABLES, CH, D])
        rest = sb("rest", [P, OH_TABLES, CH, D])
        part2 = sb("part2", [P, OH_TABLES, CH, D], bf16)
        onehot = sb("onehot", [P, OH_BUFFERS, CH, BATCH], bf16)
        distance = sb("distance", [P, CH, BATCH], bf16)
        pickedT = sb("pickedT", [P, OH_TABLES, BATCH])
        emb = sb("emb", [P, 2, OH_SLOT, D])
        XT = sb("XT", [P, P, SLOTS])
        denseT = sb("denseT", [P, P])
        Zd = sb("Zd", [P, ROWS * (WRAP + 1)])
        pairs = sb("pairs", [P, SLOTS * HALF])
        zT = sb("zT", [P, Z_CHUNKS, P])
        w1_sb = sb("w1_sb", [P, Z_CHUNKS, H1])
        w1d_sb = sb("w1d_sb", [P, 2, H1])
        w1s_sb = sb("w1s_sb", [P, H1])
        w2_sb = sb("w2_sb", [P, M1, H2])
        w3_sb = sb("w3_sb", [P, M2])
        b1_sb = sb("b1_sb", [P, M1])
        b2_sb = sb("b2_sb", [P, M2])
        h1T = sb("h1T", [P, M1, P])
        h2T = sb("h2T", [P, M2, P])
        y_row = sb("y_row", [1, BATCH])

        tab_hi = tab[:, :, :, :].bitcast(bf16).rearrange("p k c (d two) -> p k c d two", two=2)[:, :, :, :, 1]
        rest_hi = rest[:, :, :, :].bitcast(bf16).rearrange("p k c (d two) -> p k c d two", two=2)[:, :, :, :, 1]
        parts = (tab_hi, rest_hi, part2)

        bank_xt = [bank("bank_xt0"), bank("bank_xt1")]
        bank_gram = bank("bank_gram", 1024)
        bank_z = bank("bank_z")
        bank_h1 = [bank("bank_h1a"), bank("bank_h1b")]
        bank_h2 = bank("bank_h2")

        ids_loaded = sem("ids_loaded")
        ids_bc_loaded = sems("ids_bc_loaded", OH_TABLES)
        tab_loaded = sems("tab_loaded", OH_TABLES)
        w1d_loaded = sem("w1d_loaded")
        weights_loaded = sem("weights_loaded")
        dense_loaded = sems("dense_loaded", TILES)
        gathered = [sems(f"gathered{a}_", NG) for a in range(2)]
        zeroed = sem("zeroed")
        consts_ready = sem("consts_ready")
        neg_ready = sem("neg_ready")
        pad_zeroed = sem("pad_zeroed")
        picked_laid_0 = sem("picked_laid_0")
        w1s_ready = sem("w1s_ready")
        ids_spread = sem("ids_spread")
        dve_onehot = sem("dve_onehot")
        act_distance = sem("act_distance")
        act_onehot = sem("act_onehot")
        rest_ready = sem("rest_ready")
        part2_ready = sem("part2_ready")
        picked = sem("picked")
        picked_out = sem("picked_out")
        picked_laid = sem("picked_laid")
        transposed = sem("transposed")
        xt_ready = [sem("xt_ready0"), sem("xt_ready1")]
        gram_ready = sem("gram_ready")
        gram_spread = sem("gram_spread")
        pairs_ready = sem("pairs_ready")
        z_ready = sem("z_ready")
        zT_ready = sem("zT_ready")
        h1_sum = sem("h1_sum")
        h1_act = sem("h1_act")
        h1_dve = sem("h1_dve")
        h2_sum = sem("h2_sum")
        h2_act = sem("h2_act")
        h2_dve = sem("h2_dve")
        y_sum = sem("y_sum")
        y_ready = sem("y_ready")
        stored = sem("stored")

        g_dmas = [min(hi, G_TABLES) - lo for lo, hi in GROUPS]

        def wait_onehot(eng, k, half):
            if k in DVE_COMPARES:
                eng.wait_ge(dve_onehot, 2 * DVE_COMPARES.index(k) + half + 1)
            else:
                eng.wait_ge(act_onehot, ACT_COMPARES.index(k) + 1)

        def wait_onehot_buffer(eng, k):
            if k >= OH_BUFFERS:
                eng.wait_ge(picked, k - OH_BUFFERS + 1)

        block = ctx.enter_context(nc.Block())

        @block.sync
        def _(sp):
            def load_dense(t):
                sp.dma_start(emb[:, t % 2, DENSE_SLOT, :], dense[t * P:(t + 1) * P, :]).then_inc(dense_loaded[t], 16)

            def load_ids_bc(k):
                f = G_TABLES + k
                sp.dma_start(ids_bc[0:VP, k, :], ids_t[f:f + 1, :].to_broadcast((VP, BATCH))).then_inc(ids_bc_loaded[k], 16)

            def load_table(k):
                sp.dma_start(tab[0:VP, k, :, :],
                             tables[G_TABLES + k].rearrange("(p c) d -> p c d", c=CH)).then_inc(tab_loaded[k], 16)

            sp.dma_start(ids_sb[:, :, :], ids_p).then_inc(ids_loaded, 16)
            load_table(0)
            load_ids_bc(1)
            load_ids_bc(2)
            load_table(1)
            load_dense(0)
            load_table(2)
            for k in range(3, OH_TABLES):
                sp.wait_ge(rest_ready, k - 2)
                load_ids_bc(k)
                load_table(k)
            load_dense(1)
            sp.wait_ge(picked, 2)
            sp.dma_start(w1d_sb[:, :, :], w1_dense.rearrange("(a p) h -> p a h", p=P)).then_inc(w1d_loaded, 16)
            sp.dma_start(w1_sb[0:Z_ROWS, :, :], w1_pairs.rearrange("(q k) h -> k q h", k=Z_ROWS)).then_inc(weights_loaded, 16)
            sp.dma_start(w2_sb[:, :, :], w2.rearrange("(k p) h -> p k h", p=P)).then_inc(weights_loaded, 16)
            sp.dma_start(b1_sb[:, :], b1).then_inc(weights_loaded, 16)
            sp.dma_start(b2_sb[:, :], b2).then_inc(weights_loaded, 16)
            sp.dma_start(w3_sb[:, :], w3).then_inc(weights_loaded, 16)
            for t in range(2, TILES):
                sp.wait_ge(transposed, (t - 1) * NG)
                load_dense(t)
            sp.wait_ge(y_ready, TILES)
            sp.dma_start(out.rearrange("b o -> o b"), y_row[:, :]).then_inc(stored, 16)
            sp.wait_ge(stored, 16)

        @block.gpsimd
        def _(pool):
            pool.iota(row_id[:, :], pattern=[[1, CH]], base=0, channel_multiplier=CH,
                      allow_small_or_imprecise_dtypes=True).then_inc(consts_ready, 1)
            pool.memset(ident[:, :], 0.0).then_inc(zeroed, 1)
            pool.wait_ge(zeroed, 1)
            pool.affine_select(out=ident[:, :], in_=ident[:, :], compare_op=ALU.not_equal, fill=1.0,
                               base=0, pattern=[[-1, P]], channel_multiplier=1).then_inc(consts_ready, 1)
            pool.wait_ge(ids_loaded, 16)
            for t in range(TILES):
                for g, (lo, hi) in enumerate(GROUPS):
                    if t >= 2:
                        pool.wait_ge(transposed, (t - 2) * NG + g + 1)
                    for f in range(lo, min(hi, G_TABLES)):
                        pool.indirect_dma_start(
                            out=emb[:, t % 2, f, :], out_offset=None, in_=tables[f][:, :],
                            in_offset=bass.IndirectOffsetOnAxis(ap=ids_sb[:, t, f:f + 1].bitcast(u32), axis=0),
                        ).then_inc(gathered[t % 2][g], 16)

        @block.tensor
        def _(pe):
            def pick_rows(k):
                pe.wait_ge(tab_loaded[k], 16)
                if k >= 2:
                    pe.wait_ge(picked_out, k - 1)
                for n, part in enumerate(parts):
                    if n == 1:
                        pe.wait_ge(rest_ready, k + 1)
                    if n == 2:
                        pe.wait_ge(part2_ready, k + 1)
                    for c in range(CH):
                        if n == 0 and c % (CH // 2) == 0:
                            wait_onehot(pe, k, c // (CH // 2))
                        last = nc.tensor.matmul(bank_h1[k % 2][:, :], part[0:VP, k, c, :],
                                                onehot[0:VP, k % OH_BUFFERS, c, :],
                                                start=(n == 0 and c == 0), stop=(n == 2 and c == CH - 1))
                last.then_inc(picked, 1)

            def transpose_group(t, g):
                lo, hi = GROUPS[g]
                n = t * NG + g
                pe.wait_ge(gathered[t % 2][g], (t // 2 + 1) * 16 * g_dmas[g])
                if g == NG - 1:
                    pe.wait_ge(dense_loaded[t], 16)
                if n >= 2:
                    pe.wait_ge(xt_ready[g % 2], n // 2)
                for slot in range(lo, hi):
                    last = nc.tensor.transpose(bank_xt[g % 2][:, (slot - lo) * P:(slot - lo + 1) * P],
                                               emb[:, t % 2, slot, :], ident[:, :])
                last.then_inc(transposed, 1)

            def tile(t):
                more = t + 1 < TILES
                pe.wait_ge(xt_ready[0], (t + 1) * (NG // 2))
                pe.wait_ge(xt_ready[1], (t + 1) * (NG // 2))
                pe.wait_ge(picked_laid, t + 1)
                if t:
                    pe.wait_ge(gram_spread, t)
                else:
                    pe.wait_ge(picked_laid_0, 1)
                for i in range(P // QUADS):
                    for s in range(QUADS):
                        b = s * ROWS + i
                        last = nc.tensor.matmul(bank_gram[s * ROWS:s * ROWS + SLOTS, i * ROWS:i * ROWS + SLOTS],
                                                XT[:, b, :], XT[:, b, :], start=True, stop=True)
                last.then_inc(gram_ready, 1)
                pe.wait_ge(w1s_ready, 1)
                if t:
                    pe.wait_ge(h1_act, t)
                    pe.wait_ge(h1_dve, t)
                else:
                    pe.wait_ge(picked_out, OH_TABLES)
                sums = [bank_h1[m // 2][:, (m % 2) * P:(m % 2 + 1) * P] for m in range(M1)]
                for m in range(M1):
                    nc.tensor.matmul(sums[m], w1s_sb[:, m * P:(m + 1) * P], denseT[:, :],
                                     start=(m % 2 == 0), stop=False, skip_group_check=True)
                if more:
                    transpose_group(t + 1, 0)
                    transpose_group(t + 1, 1)
                pe.wait_ge(pairs_ready, t + 1)
                if t:
                    pe.wait_ge(h2_act, t)
                for q in range(Z_CHUNKS):
                    last = nc.tensor.transpose(bank_z[0:Z_ROWS, q * P:(q + 1) * P],
                                               pairs[:, q * Z_ROWS:(q + 1) * Z_ROWS], ident[:, :])
                last.then_inc(z_ready, 1)
                if more:
                    transpose_group(t + 1, 2)
                    transpose_group(t + 1, 3)
                pe.wait_ge(zT_ready, t + 1)
                pe.wait_ge(weights_loaded, 16 * 5)
                for m in range(M1):
                    for q in range(Z_CHUNKS):
                        last = nc.tensor.matmul(sums[m], w1_sb[0:Z_ROWS, q, m * P:(m + 1) * P], zT[0:Z_ROWS, q, :],
                                                start=False, stop=(q == Z_CHUNKS - 1), skip_group_check=True)
                    if m % 2:
                        last.then_inc(h1_sum, 1)
                if t:
                    pe.wait_ge(h2_dve, t)
                    pe.wait_ge(y_ready, t)
                for half in range(2):
                    pe.wait_ge((h1_act, h1_dve)[half], t + 1)
                    for m in range(M2):
                        for k in range(2 * half, 2 * half + 2):
                            last = nc.tensor.matmul((bank_z, bank_h2)[m][:, 0:P], w2_sb[:, k, m * P:(m + 1) * P],
                                                    h1T[:, k, :], start=(k == 0), stop=(k == M1 - 1))
                        if half:
                            last.then_inc(h2_sum, 1)
                if more:
                    transpose_group(t + 1, 4)
                    transpose_group(t + 1, 5)
                pe.wait_ge(h2_act, t + 1)
                pe.wait_ge(h2_dve, t + 1)
                for k in range(M2):
                    last = nc.tensor.matmul(bank_h2[0:1, 2 * P:3 * P], w3_sb[:, k:k + 1], h2T[:, k, :],
                                            start=(k == 0), stop=(k == M2 - 1))
                last.then_inc(y_sum, 1)

            pe.wait_ge(consts_ready, 2)
            after = {0: (0,), 1: (1, 2), 2: (3, 4), 3: (5,)}
            for k in range(OH_TABLES):
                pick_rows(k)
                for g in after.get(k, ()):
                    transpose_group(0, g)
            for t in range(TILES):
                tile(t)

        @block.vector
        def _(dve):
            def compare(k):
                n = DVE_COMPARES.index(k)
                dve.wait_ge(ids_spread, n + 1)
                wait_onehot_buffer(dve, k)
                ids = bank_gram[0:VP, (n % 2) * BATCH:(n % 2 + 1) * BATCH].rearrange("p (a b) -> p a b", a=1)
                for c in (0, CH // 2):
                    rows = row_id[0:VP, c:c + CH // 2].rearrange("p (c a) -> p c a", a=1)
                    nc.vector.tensor_tensor(
                        onehot[0:VP, k % OH_BUFFERS, c:c + CH // 2, :], ids.to_broadcast((VP, CH // 2, BATCH)),
                        rows.to_broadcast((VP, CH // 2, BATCH)), ALU.is_equal).then_inc(dve_onehot, 1)

            def split(k):
                dve.wait_ge(tab_loaded[k], 16)
                nc.vector.tensor_tensor(rest[0:VP, k, :, :], tab[0:VP, k, :, :], tab_hi[0:VP, k, :, :],
                                        ALU.subtract).then_inc(rest_ready, 1)
                dve.wait_ge(rest_ready, k + 1)
                nc.vector.tensor_tensor(part2[0:VP, k, :, :], rest[0:VP, k, :, :], rest_hi[0:VP, k, :, :],
                                        ALU.subtract).then_inc(part2_ready, 1)

            def lay_group(t, g):
                lo, hi = GROUPS[g]
                dve.wait_ge(transposed, t * NG + g + 1)
                nc.vector.tensor_copy(XT[:, :, lo:hi].rearrange("p b s -> p s b"),
                                      bank_xt[0][:, 0:(hi - lo) * P].rearrange("p (s b) -> p s b", b=P)
                                      ).then_inc(xt_ready[0], 1)

            def tile(t):
                more = t + 1 < TILES
                dve.wait_ge(gram_ready, t + 1)
                gram = bank_gram[:, :].rearrange("p (i c) -> p c i", c=ROWS)
                zd = Zd[:, 0:ROWS * WRAP].rearrange("p (r c) -> p c r", c=WRAP)
                nc.vector.transpose(zd[:, 0:SLOTS, :], gram[:, 0:SLOTS, :])
                nc.vector.transpose(zd[:, SLOTS:WRAP, :], gram[:, 0:HALF, :]).then_inc(gram_spread, 1)
                dve.wait_ge(gram_spread, t + 1)
                if t:
                    dve.wait_ge(z_ready, t)
                nc.vector.tensor_copy(pairs[:, :].rearrange("p (j s) -> p j s", s=HALF),
                                      Zd[:, :].rearrange("p (r c) -> p r c", c=WRAP + 1)[:, 0:SLOTS, 1:1 + HALF]
                                      ).then_inc(pairs_ready, 1)
                if more:
                    lay_group(t + 1, 0)
                    lay_group(t + 1, 2)
                dve.wait_ge(h1_sum, t * 2 + 2)
                for m in range(M1 // 2, M1):
                    last = nc.vector.tensor_scalar(h1T[:, m, :], bank_h1[1][:, (m % 2) * P:(m % 2 + 1) * P],
                                                   b1_sb[:, m:m + 1], 0.0, ALU.add, ALU.max)
                last.then_inc(h1_dve, 1)
                dve.wait_ge(h2_sum, t * 2 + 2)
                nc.vector.tensor_scalar(h2T[:, 1, :], bank_h2[:, 0:P], b2_sb[:, 1:2], 0.0,
                                        ALU.add, ALU.max).then_inc(h2_dve, 1)
                if more:
                    lay_group(t + 1, 4)

            dve.wait_ge(consts_ready, 1)
            nc.vector.tensor_scalar(neg_row_id[:, :], row_id[:, :], -1.0, None, ALU.mult).then_inc(neg_ready, 1)
            nc.vector.memset(bank_gram[:, :], 0.0).then_inc(pad_zeroed, 1)
            compare(0)
            split(0)
            split(1)
            compare(2)
            lay_group(0, 0)
            split(2)
            compare(3)
            lay_group(0, 2)
            split(3)
            split(4)
            lay_group(0, 4)
            compare(5)
            split(5)
            dve.wait_ge(w1d_loaded, 16)
            nc.vector.tensor_tensor(w1s_sb[:, :], w1d_sb[:, 0, :], w1d_sb[:, 1, :], ALU.add).then_inc(w1s_ready, 1)
            dve.wait_ge(weights_loaded, 16 * 5)
            for t in range(TILES):
                tile(t)

        @block.scalar
        def _(act):
            def spread_ids(k):
                n = DVE_COMPARES.index(k)
                act.wait_ge(ids_bc_loaded[k], 16)
                if n >= 2:
                    act.wait_ge(dve_onehot, 2 * (n - 1))
                nc.scalar.copy(bank_gram[0:VP, (n % 2) * BATCH:(n % 2 + 1) * BATCH],
                               ids_bc[0:VP, k, :]).then_inc(ids_spread, 1)

            def measure(k):
                n = ACT_COMPARES.index(k)
                act.wait_ge(ids_bc_loaded[k], 16)
                act.wait_ge(neg_ready, 1)
                if n:
                    act.wait_ge(act_onehot, n)
                for c in range(CH):
                    nc.scalar.activation(distance[0:VP, c, :], ids_bc[0:VP, k, :], ACT.Square,
                                         bias=neg_row_id[0:VP, c:c + 1]).then_inc(act_distance, 1)

            def compare(k):
                n = ACT_COMPARES.index(k)
                act.wait_ge(act_distance, (n + 1) * CH)
                wait_onehot_buffer(act, k)
                nc.scalar.activation(onehot[0:VP, k % OH_BUFFERS, :, :], distance[0:VP, :, :], ACT.Relu,
                                     bias=1.0, scale=-1.0).then_inc(act_onehot, 1)

            def take_picked(k):
                act.wait_ge(picked, k + 1)
                nc.scalar.copy(pickedT[:, k, :], bank_h1[k % 2][:, :]).then_inc(picked_out, 1)

            def lay_picked(t, tables, src, done):
                if t:
                    act.wait_ge(gram_ready, t)
                nc.scalar.copy(XT[:, :, OH_SLOT + tables[0]:OH_SLOT + tables[1]].rearrange("p b s -> p s b"),
                               src).then_inc(done, 1)

            def lay_picked_tile(t):
                act.wait_ge(picked_out, OH_TABLES)
                lay_picked(t, (0, OH_TABLES), pickedT[:, :, t * P:(t + 1) * P], picked_laid)

            def lay_group(t, g):
                lo, hi = GROUPS[g]
                act.wait_ge(transposed, t * NG + g + 1)
                if g == NG - 1:
                    nc.scalar.copy(denseT[:, :], bank_xt[1][:, (DENSE_SLOT - lo) * P:(DENSE_SLOT - lo + 1) * P])
                nc.scalar.copy(XT[:, :, lo:hi].rearrange("p b s -> p s b"),
                               bank_xt[1][:, 0:(hi - lo) * P].rearrange("p (s b) -> p s b", b=P)
                               ).then_inc(xt_ready[1], 1)

            def tile(t):
                more = t + 1 < TILES
                if more:
                    lay_picked_tile(t + 1)
                    lay_group(t + 1, 1)
                act.wait_ge(z_ready, t + 1)
                nc.scalar.copy(zT[0:Z_ROWS, :, :].rearrange("p q b -> p (q b)"),
                               bank_z[0:Z_ROWS, 0:Z_CHUNKS * P]).then_inc(zT_ready, 1)
                if more:
                    lay_group(t + 1, 3)
                act.wait_ge(h1_sum, t * 2 + 1)
                for m in range(M1 // 2):
                    last = nc.scalar.activation(h1T[:, m, :], bank_h1[0][:, m * P:(m + 1) * P], ACT.Relu,
                                                bias=b1_sb[:, m:m + 1])
                last.then_inc(h1_act, 1)
                act.wait_ge(h2_sum, t * 2 + 1)
                nc.scalar.activation(h2T[:, 0, :], bank_z[:, 0:P], ACT.Relu, bias=b2_sb[:, 0:1]).then_inc(h2_act, 1)
                if more:
                    lay_group(t + 1, 5)
                act.wait_ge(y_sum, t + 1)
                nc.scalar.copy(y_row[:, t * P:(t + 1) * P], bank_h2[0:1, 2 * P:3 * P]).then_inc(y_ready, 1)

            act.dma_start(ids_bc[0:VP, 0, :], ids_t[G_TABLES:G_TABLES + 1, :].to_broadcast((VP, BATCH))
                          ).then_inc(ids_bc_loaded[0], 16)
            act.wait_ge(pad_zeroed, 1)
            spread_ids(0)
            measure(1)
            spread_ids(2)
            compare(1)
            spread_ids(3)
            take_picked(0)
            measure(4)
            take_picked(1)
            compare(4)
            lay_group(0, 1)
            spread_ids(5)
            take_picked(2)
            lay_group(0, 3)
            take_picked(3)
            lay_group(0, 5)
            take_picked(4)
            last = OH_TABLES - 1
            act.wait_ge(picked_out, last)
            lay_picked(0, (0, last), pickedT[:, 0:last, 0:P], picked_laid_0)
            act.wait_ge(picked, OH_TABLES)
            lay_picked(0, (last, last + 1), bank_h1[last % 2][:, 0:P].rearrange("p (s b) -> p s b", s=1), picked_laid)
            take_picked(last)
            act.wait_ge(weights_loaded, 16 * 5)
            for t in range(TILES):
                tile(t)


def pair_rows():
    feature = list(range(1, 1 + G_TABLES)) + [0] + list(range(1 + G_TABLES, SLOTS))
    order = []
    for j in range(SLOTS):
        for step in range(1, HALF + 1):
            a, b = sorted((feature[j], feature[(j + step) % SLOTS]))
            order.append(D + a * (2 * SLOTS - a - 1) // 2 + (b - a - 1))
    return order


def kernel(**inputs):
    import numpy as np
    import concourse.bacc as bacc
    from concourse import mybir as mb
    from concourse.bass_utils import run_bass_kernel_spmd

    ids = np.asarray(inputs["ids"])
    w1 = np.asarray(inputs["W_top1"])
    n_pairs = SLOTS * HALF
    laid = {
        "dense": np.asarray(inputs["r_dense_features"]),
        "ids_p": ids.reshape(TILES, P, NF).transpose(1, 0, 2),
        "ids_t": ids.transpose(),
        "w1_pairs": w1[np.array(pair_rows())],
        "w1_dense": np.concatenate([w1[0:D], w1[D + n_pairs:]]),
        "b1": np.asarray(inputs["b_top1"]).reshape(M1, P).transpose(),
        "w2": np.asarray(inputs["W_top2"]),
        "b2": np.asarray(inputs["b_top2"]).reshape(M2, P).transpose(),
        "w3": np.asarray(inputs["W_top3"]).reshape(M2, P).transpose(),
    }
    for f in range(NF):
        laid[f"tbl_{f}"] = np.asarray(inputs[f"tbl_{f}"])

    nc = bacc.Bacc("TRN2", target_bir_lowering=False, num_devices=1)
    arrays, args = {}, {}
    for name, a in laid.items():
        a = np.ascontiguousarray(a)
        arrays[f"in_{name}"] = a
        args[name] = nc.dram_tensor(f"in_{name}", a.shape, mb.dt.from_np(a.dtype), kind="ExternalInput").ap()
    out = nc.dram_tensor("out_y", (BATCH, 1), mb.dt.float32, kind="ExternalOutput").ap()
    tables = [args.pop(f"tbl_{f}") for f in range(NF)]
    dlrm_tower(nc, tables=tables, out=out, **args)
    result = run_bass_kernel_spmd(nc, [arrays], core_ids=[0])
    return result.results[0]["out_y"]
```

```python
import concourse.bass as bass
from concourse import mybir
from contextlib import ExitStack

P = 128
NF = 26
D = 128
BATCH = 512
TILES = BATCH // P
SLOTS = NF + 1
ROWS = 32
QUADS = 4
HALF = (SLOTS - 1) // 2
Z_CHUNKS = 3
Z_RUNS = SLOTS // Z_CHUNKS
Z_ROWS = Z_RUNS * HALF
WRAP = SLOTS + HALF
H1, H2 = 512, 256
M1, M2 = H1 // P, H2 // P

PICKED = list(range(19, 26)) + [13, 12]
FROM = [0] * 7 + [1, 2]
GATHERED = [f for f in range(NF) if f not in PICKED]
OH_TABLES = len(PICKED)
EARLY = FROM.count(0)
G_TABLES = len(GATHERED)
DENSE_SLOT = G_TABLES
OH_SLOT = G_TABLES + 1
VOCAB = 1000
CH = 8
VP = VOCAB // CH
DVE_CH = 6
ACT_CH = CH - DVE_CH
RING = 3

GROUPS = [(0, 4), (4, 8), (8, 11), (11, 14), (14, 16), (16, 18)]
NG = len(GROUPS)
assert GROUPS[-1][1] == OH_SLOT


def gathered_late(t):
    return sum(first > t for first in FROM)


def group(t, g):
    lo, hi = GROUPS[g]
    return lo, hi + (gathered_late(t) if g == NG - 1 else 0)


def oh_index(k):
    late = OH_TABLES - EARLY
    return k + late if k < EARLY else OH_TABLES - 1 - k


def gathers(t, g):
    tables = dict(enumerate(GATHERED))
    tables.update((OH_SLOT + oh_index(k), PICKED[k]) for k in range(EARLY, OH_TABLES))
    lo, hi = group(t, g)
    return [(slot, tables[slot]) for slot in range(lo, hi) if slot != DENSE_SLOT]


def dlrm_tower(nc, dense, ids_p, ids_t, tables, w1_pairs, w1_dense, b1, w2, b2, w3, out):
    f32, f32r, i32, u32 = mybir.dt.float32, mybir.dt.float32r, mybir.dt.int32, mybir.dt.uint32
    ALU, ACT = mybir.AluOpType, mybir.ActivationFunctionType

    with ExitStack() as ctx:
        def sb(name, shape, dt=f32):
            return ctx.enter_context(nc.sbuf_tensor(name, shape, dt))

        def bank(name, cols=512):
            return ctx.enter_context(nc.psum_tensor(name, [P, cols], f32))

        def sem(name):
            return ctx.enter_context(nc.semaphore(name))

        def sems(name, n):
            return [sem(f"{name}{i}") for i in range(n)]

        ident = sb("ident", [P, P])
        row_id = sb("row_id", [P, CH])
        neg_row_id = sb("neg_row_id", [P, CH])
        ids_sb = sb("ids_sb", [P, TILES, NF], i32)
        ids_bc = sb("ids_bc", [P, RING, BATCH], i32)
        tab = sb("tab", [P, RING, CH, D])
        tab_hi = sb("tab_hi", [P, RING, CH, D], f32r)
        tab_lo = sb("tab_lo", [P, RING, CH, D], f32r)
        onehot = sb("onehot", [P, RING, CH, BATCH], f32r)
        distance = sb("distance", [P, RING, ACT_CH, BATCH])
        pickedT = sb("pickedT", [P, OH_TABLES, BATCH])
        emb = sb("emb", [P, 2, OH_SLOT + OH_TABLES - EARLY, D])
        XT = sb("XT", [P, P, SLOTS])
        denseT = sb("denseT", [P, P])
        Zd = sb("Zd", [P, ROWS * (WRAP + 1)])
        pairs = sb("pairs", [P, SLOTS * HALF])
        zT = sb("zT", [P, Z_CHUNKS, P])
        w1_sb = sb("w1_sb", [P, Z_CHUNKS, H1])
        w1d_sb = sb("w1d_sb", [P, 2, H1])
        w1s_sb = sb("w1s_sb", [P, H1])
        w2_sb = sb("w2_sb", [P, M1, H2])
        w3_sb = sb("w3_sb", [P, M2])
        b1_sb = sb("b1_sb", [P, M1])
        b2_sb = sb("b2_sb", [P, M2])
        h1T = sb("h1T", [P, M1, P])
        h2T = sb("h2T", [P, M2, P])
        y_row = sb("y_row", [1, BATCH])

        bank_xt = [bank("bank_xt0"), bank("bank_xt1")]
        bank_gram = bank("bank_gram", 1024)
        bank_z = bank("bank_z")
        bank_h1 = [bank("bank_h1a"), bank("bank_h1b")]
        bank_h2 = bank("bank_h2")
        bank_zq = [bank_z, bank_h2, bank_z]

        ids_loaded = sem("ids_loaded")
        ids_bc_loaded = sems("ids_bc_loaded", OH_TABLES)
        tab_loaded = sems("tab_loaded", OH_TABLES)
        w1d_loaded = sem("w1d_loaded")
        weights_loaded = sem("weights_loaded")
        dense_loaded = sems("dense_loaded", TILES)
        gathered = [sems(f"gathered{a}_", NG) for a in range(2)]
        zeroed = sem("zeroed")
        consts_ready = sem("consts_ready")
        neg_ready = sem("neg_ready")
        pad_zeroed = sem("pad_zeroed")
        picked_laid_0 = sem("picked_laid_0")
        w1s_ready = sem("w1s_ready")
        ids_spread = sem("ids_spread")
        hi_ready = sem("hi_ready")
        lo_ready = sem("lo_ready")
        dve_onehot = sem("dve_onehot")
        act_distance = sem("act_distance")
        act_onehot = sem("act_onehot")
        picked = sem("picked")
        picked_out = sem("picked_out")
        picked_laid = sem("picked_laid")
        transposed = sem("transposed")
        xt_ready = [sem("xt_ready0"), sem("xt_ready1")]
        gram_ready = sem("gram_ready")
        gram_spread = sem("gram_spread")
        pairs_ready = sem("pairs_ready")
        z_ready = sem("z_ready")
        zT_ready = sem("zT_ready")
        h1_sum = sem("h1_sum")
        h1_act = sem("h1_act")
        h1_dve = sem("h1_dve")
        h2_sum = sem("h2_sum")
        h2_act = sem("h2_act")
        h2_dve = sem("h2_dve")
        y_sum = sem("y_sum")
        y_ready = sem("y_ready")
        stored = sem("stored")

        def columns(k):
            return slice(P * FROM[k], BATCH)

        def ids_bank(k):
            return bank_h2[:, :] if k >= EARLY else bank_gram[:, (k % 2) * BATCH:(k % 2 + 1) * BATCH]

        def wait_ring(eng, k):
            if k >= RING:
                eng.wait_ge(picked, k - RING + 1)

        block = ctx.enter_context(nc.Block())

        @block.sync
        def _(sp):
            def load_dense(t):
                sp.dma_start(emb[:, t % 2, DENSE_SLOT, :], dense[t * P:(t + 1) * P, :]).then_inc(dense_loaded[t], 16)

            def load_ids_bc(k):
                f = PICKED[k]
                sp.dma_start(ids_bc[0:VP, k % RING, :],
                             ids_t[f:f + 1, :].to_broadcast((VP, BATCH))).then_inc(ids_bc_loaded[k], 16)

            def load_table(k):
                sp.dma_start(tab[0:VP, k % RING, :, :],
                             tables[PICKED[k]].rearrange("(p c) d -> p c d", c=CH)).then_inc(tab_loaded[k], 16)

            sp.dma_start(ids_sb[:, :, :], ids_p).then_inc(ids_loaded, 16)
            load_table(0)
            load_ids_bc(1)
            load_ids_bc(2)
            load_table(1)
            load_dense(0)
            load_table(2)
            for k in range(3, OH_TABLES):
                sp.wait_ge(act_onehot, k - RING + 1)
                sp.wait_ge(dve_onehot, 2 * (k - RING + 1))
                load_ids_bc(k)
                sp.wait_ge(lo_ready, k - RING + 1)
                load_table(k)
            load_dense(1)
            sp.wait_ge(picked, 2)
            sp.dma_start(w1d_sb[:, :, :], w1_dense.rearrange("(a p) h -> p a h", p=P)).then_inc(w1d_loaded, 16)
            sp.dma_start(w1_sb[0:Z_ROWS, :, :],
                         w1_pairs.rearrange("(q k) h -> k q h", k=Z_ROWS)).then_inc(weights_loaded, 16)
            sp.dma_start(w2_sb[:, :, :], w2.rearrange("(k p) h -> p k h", p=P)).then_inc(weights_loaded, 16)
            sp.dma_start(b1_sb[:, :], b1).then_inc(weights_loaded, 16)
            sp.dma_start(b2_sb[:, :], b2).then_inc(weights_loaded, 16)
            sp.dma_start(w3_sb[:, :], w3).then_inc(weights_loaded, 16)
            for t in range(2, TILES):
                sp.wait_ge(transposed, (t - 1) * NG)
                load_dense(t)
            sp.wait_ge(y_ready, TILES)
            sp.dma_start(out.rearrange("b o -> o b"), y_row[:, :]).then_inc(stored, 16)
            sp.wait_ge(stored, 16)

        @block.gpsimd
        def _(pool):
            pool.iota(row_id[:, :], pattern=[[1, CH]], base=0, channel_multiplier=CH,
                      allow_small_or_imprecise_dtypes=True).then_inc(consts_ready, 1)
            pool.memset(ident[:, :], 0.0).then_inc(zeroed, 1)
            pool.wait_ge(zeroed, 1)
            pool.affine_select(out=ident[:, :], in_=ident[:, :], compare_op=ALU.not_equal, fill=1.0,
                               base=0, pattern=[[-1, P]], channel_multiplier=1).then_inc(consts_ready, 1)
            pool.wait_ge(ids_loaded, 16)
            for t in range(TILES):
                for g in range(NG):
                    if t >= 2:
                        pool.wait_ge(transposed, (t - 2) * NG + g + 1)
                    for slot, f in gathers(t, g):
                        pool.indirect_dma_start(
                            out=emb[:, t % 2, slot, :], out_offset=None, in_=tables[f][:, :],
                            in_offset=bass.IndirectOffsetOnAxis(ap=ids_sb[:, t, f:f + 1].bitcast(u32), axis=0),
                        ).then_inc(gathered[t % 2][g], 16)

        @block.tensor
        def _(pe):
            def pick_rows(k):
                if k >= 2:
                    pe.wait_ge(picked_out, k - 1)
                for n, part in enumerate((tab_hi, tab_lo)):
                    pe.wait_ge((hi_ready, lo_ready)[n], k + 1)
                    for c in range(CH):
                        if n == 0 and c == 0:
                            pe.wait_ge(dve_onehot, 2 * k + 1)
                        if n == 0 and c == DVE_CH // 2:
                            pe.wait_ge(dve_onehot, 2 * k + 2)
                        if n == 0 and c == DVE_CH:
                            pe.wait_ge(act_onehot, k + 1)
                        last = nc.tensor.matmul(bank_h1[k % 2][:, columns(k)], part[0:VP, k % RING, c, :],
                                                onehot[0:VP, k % RING, c, columns(k)],
                                                start=(n == 0 and c == 0), stop=(n == 1 and c == CH - 1))
                last.then_inc(picked, 1)

            def transpose_group(t, g):
                lo, hi = group(t, g)
                n = t * NG + g
                pe.wait_ge(gathered[t % 2][g], 16 * sum(len(gathers(u, g)) for u in range(t % 2, t + 1, 2)))
                if g == NG - 1:
                    pe.wait_ge(dense_loaded[t], 16)
                if n >= 2:
                    pe.wait_ge(xt_ready[g % 2], n // 2)
                for slot in range(lo, hi):
                    last = nc.tensor.transpose(bank_xt[g % 2][:, (slot - lo) * P:(slot - lo + 1) * P],
                                               emb[:, t % 2, slot, :], ident[:, :])
                last.then_inc(transposed, 1)

            def turn_pairs(t, q):
                pe.wait_ge(pairs_ready, t * Z_CHUNKS + q + 1)
                if q == 2:
                    pe.wait_ge(zT_ready, t * Z_CHUNKS + 1)
                nc.tensor.transpose(bank_zq[q][0:Z_ROWS, 0:P],
                                    pairs[:, q * Z_ROWS:(q + 1) * Z_ROWS], ident[:, :]).then_inc(z_ready, 1)

            def dense_layer(t, sums):
                pe.wait_ge(w1s_ready, 1)
                if t:
                    pe.wait_ge(h1_act, 2 * t)
                    pe.wait_ge(h1_dve, 2 * t)
                for m in range(M1):
                    if m % 2 == 0 and EARLY + t < OH_TABLES:
                        pe.wait_ge(picked_out, EARLY + t + (m // 2 == (EARLY + t) % 2))
                    nc.tensor.matmul(sums[m], w1s_sb[:, m * P:(m + 1) * P], denseT[:, :],
                                     start=(m % 2 == 0), stop=False, skip_group_check=True)

            def tile(t):
                more = t + 1 < TILES
                pe.wait_ge(xt_ready[0], (t + 1) * (NG // 2))
                pe.wait_ge(xt_ready[1], (t + 1) * (NG // 2))
                pe.wait_ge(picked_laid, t + 1)
                if t:
                    pe.wait_ge(gram_spread, 2 * t)
                else:
                    pe.wait_ge(picked_laid_0, 1)
                for i in range(P // QUADS):
                    for s in range(QUADS):
                        b = s * ROWS + i
                        last = nc.tensor.matmul(bank_gram[s * ROWS:s * ROWS + SLOTS, i * ROWS:i * ROWS + SLOTS],
                                                XT[:, b, :], XT[:, b, :], start=True, stop=True)
                last.then_inc(gram_ready, 1)
                if t:
                    third_layer(t - 1)
                sums = [bank_h1[m // 2][:, (m % 2) * P:(m % 2 + 1) * P] for m in range(M1)]
                late = EARLY + t < OH_TABLES
                if late:
                    if t:
                        pe.wait_ge(h1_act, 2 * t)
                        pe.wait_ge(h1_dve, 2 * t)
                    pick_rows(EARLY + t)
                else:
                    dense_layer(t, sums)
                if more and t:
                    transpose_group(t + 1, 0)
                if t:
                    pe.wait_ge(h2_act, t)
                    pe.wait_ge(h2_dve, t)
                    pe.wait_ge(y_ready, t)
                turn_pairs(t, 0)
                if more:
                    transpose_group(t + 1, 1)
                turn_pairs(t, 1)
                if late:
                    dense_layer(t, sums)
                pe.wait_ge(weights_loaded, 16 * 5)
                for q in range(Z_CHUNKS):
                    pe.wait_ge(zT_ready, t * Z_CHUNKS + q + 1)
                    for m in range(M1):
                        last = nc.tensor.matmul(sums[m], w1_sb[0:Z_ROWS, q, m * P:(m + 1) * P], zT[0:Z_ROWS, q, :],
                                                start=False, stop=(q == Z_CHUNKS - 1), skip_group_check=True)
                        if q == Z_CHUNKS - 1 and m % 2:
                            last.then_inc(h1_sum, 1)
                    if q == 0:
                        turn_pairs(t, 2)
                    if q == 1 and more:
                        transpose_group(t + 1, 2)
                if more:
                    transpose_group(t + 1, 3)

                def second_layer(k, m):
                    return nc.tensor.matmul((bank_z, bank_h2)[m][:, 0:P], w2_sb[:, k, m * P:(m + 1) * P],
                                            h1T[:, k, :], start=(k == 0), stop=(k == M1 - 1))

                for k in range(2):
                    pe.wait_ge(h1_act, 2 * t + k + 1)
                    for m in range(M2):
                        second_layer(k, m)
                if more:
                    transpose_group(t + 1, 4)
                    transpose_group(t + 1, 5)
                pe.wait_ge(h1_dve, 2 * t + 2)
                for m in range(M2):
                    for k in range(2, M1):
                        last = second_layer(k, m)
                    last.then_inc(h2_sum, 1)

            def third_layer(t):
                for k in range(M2):
                    pe.wait_ge((h2_act, h2_dve)[k], t + 1)
                    last = nc.tensor.matmul(bank_z[0:1, 2 * P:3 * P], w3_sb[:, k:k + 1], h2T[:, k, :],
                                            start=(k == 0), stop=(k == M2 - 1))
                last.then_inc(y_sum, 1)

            pe.wait_ge(consts_ready, 2)
            after = {1: (0,), 2: (1,), 3: (2, 3), 4: (4, 5)}
            for k in range(EARLY):
                pick_rows(k)
                for g in after.get(k, ()):
                    transpose_group(0, g)
            transpose_group(1, 0)
            for t in range(TILES):
                tile(t)
            third_layer(TILES - 1)

        @block.vector
        def _(dve):
            def compare(k):
                dve.wait_ge(ids_spread, k + 1)
                wait_ring(dve, k)
                n = DVE_CH // 2
                cols = columns(k)
                size = cols.stop - cols.start
                ids = ids_bank(k)[0:VP, cols].rearrange("p (a b) -> p a b", a=1)
                for c in (0, n):
                    rows = row_id[0:VP, c:c + n].rearrange("p (c a) -> p c a", a=1)
                    nc.vector.tensor_tensor(onehot[0:VP, k % RING, c:c + n, cols], ids.to_broadcast((VP, n, size)),
                                            rows.to_broadcast((VP, n, size)), ALU.is_equal).then_inc(dve_onehot, 1)

            def take_lo(k):
                dve.wait_ge(hi_ready, k + 1)
                nc.vector.tensor_tensor(tab_lo[0:VP, k % RING, :, :], tab[0:VP, k % RING, :, :],
                                        tab_hi[0:VP, k % RING, :, :].bitcast(f32), ALU.subtract).then_inc(lo_ready, 1)

            def lay_group(t, g):
                lo, hi = GROUPS[g]
                dve.wait_ge(transposed, t * NG + g + 1)
                nc.vector.tensor_copy(XT[:, :, lo:hi].rearrange("p b s -> p s b"),
                                      bank_xt[0][:, 0:(hi - lo) * P].rearrange("p (s b) -> p s b", b=P)
                                      ).then_inc(xt_ready[0], 1)

            def tile(t):
                more = t + 1 < TILES
                dve.wait_ge(gram_ready, t + 1)
                gram = bank_gram[:, :].rearrange("p (i c) -> p c i", c=ROWS)
                zd = Zd[:, 0:ROWS * WRAP].rearrange("p (r c) -> p c r", c=WRAP)
                nc.vector.transpose(zd[:, 0:SLOTS, :], gram[:, 0:SLOTS, :]).then_inc(gram_spread, 1)
                for q in range(Z_CHUNKS):
                    dve.wait_ge(gram_spread, 2 * t + min(q, 1) + 1)
                    if t:
                        dve.wait_ge(z_ready, (t - 1) * Z_CHUNKS + q + 1)
                    runs = slice(q * Z_RUNS, (q + 1) * Z_RUNS)
                    nc.vector.tensor_copy(pairs[:, :].rearrange("p (j s) -> p j s", s=HALF)[:, runs, :],
                                          Zd[:, :].rearrange("p (r c) -> p r c", c=WRAP + 1)[:, runs, 1:1 + HALF]
                                          ).then_inc(pairs_ready, 1)
                    if q == 0:
                        nc.vector.transpose(zd[:, SLOTS:WRAP, :], gram[:, 0:HALF, :]).then_inc(gram_spread, 1)
                if more:
                    lay_group(t + 1, 0)
                    lay_group(t + 1, 2)
                dve.wait_ge(h1_sum, t * 2 + 2)
                for m in range(M1 // 2, M1):
                    nc.vector.tensor_scalar(h1T[:, m, :], bank_h1[1][:, (m % 2) * P:(m % 2 + 1) * P],
                                            b1_sb[:, m:m + 1], 0.0, ALU.add, ALU.max).then_inc(h1_dve, 1)
                if more:
                    lay_group(t + 1, 4)
                dve.wait_ge(h2_sum, t * 2 + 2)
                nc.vector.tensor_scalar(h2T[:, 1, :], bank_h2[:, 0:P], b2_sb[:, 1:2], 0.0,
                                        ALU.add, ALU.max).then_inc(h2_dve, 1)
                if EARLY + t + 1 < OH_TABLES:
                    compare(EARLY + t + 1)
                    take_lo(EARLY + t + 1)

            nc.vector.memset(bank_gram[:, :], 0.0).then_inc(pad_zeroed, 1)
            dve.wait_ge(consts_ready, 1)
            after = {2: 0, 4: 2, 6: 4}
            for k in range(EARLY + 1):
                compare(k)
                take_lo(k)
                if k in after:
                    lay_group(0, after[k])
            dve.wait_ge(w1d_loaded, 16)
            nc.vector.tensor_tensor(w1s_sb[:, :], w1d_sb[:, 0, :], w1d_sb[:, 1, :], ALU.add).then_inc(w1s_ready, 1)
            dve.wait_ge(weights_loaded, 16 * 5)
            for t in range(TILES):
                tile(t)

        @block.scalar
        def _(act):
            def spread_ids(k):
                act.wait_ge(ids_bc_loaded[k], 16)
                if 2 <= k < EARLY:
                    act.wait_ge(dve_onehot, 2 * (k - 1))
                if k > EARLY:
                    act.wait_ge(h2_dve, k - EARLY)
                nc.scalar.copy(ids_bank(k)[0:VP, columns(k)],
                               ids_bc[0:VP, k % RING, columns(k)]).then_inc(ids_spread, 1)

            def take_hi(k):
                act.wait_ge(tab_loaded[k], 16)
                wait_ring(act, k)
                nc.scalar.copy(tab_hi[0:VP, k % RING, :, :], tab[0:VP, k % RING, :, :]).then_inc(hi_ready, 1)

            def compare(k):
                for c in range(ACT_CH):
                    nc.scalar.activation(distance[0:VP, k % RING, c, columns(k)],
                                         ids_bc[0:VP, k % RING, columns(k)], ACT.Square,
                                         bias=neg_row_id[0:VP, DVE_CH + c:DVE_CH + c + 1]).then_inc(act_distance, 1)
                act.wait_ge(act_distance, (k + 1) * ACT_CH)
                nc.scalar.activation(onehot[0:VP, k % RING, DVE_CH:CH, columns(k)],
                                     distance[0:VP, k % RING, :, columns(k)], ACT.Relu,
                                     bias=1.0, scale=-1.0).then_inc(act_onehot, 1)

            def take_picked(k):
                act.wait_ge(picked, k + 1)
                nc.scalar.copy(pickedT[:, oh_index(k), columns(k)],
                               bank_h1[k % 2][:, columns(k)]).then_inc(picked_out, 1)

            def lay_picked(t, tables, src, done):
                if t:
                    act.wait_ge(gram_ready, t)
                nc.scalar.copy(XT[:, :, OH_SLOT + tables[0]:OH_SLOT + tables[1]].rearrange("p b s -> p s b"),
                               src).then_inc(done, 1)

            def lay_picked_tile(t):
                first = gathered_late(t)
                act.wait_ge(picked_out, OH_TABLES - first)
                lay_picked(t, (first, OH_TABLES), pickedT[:, first:OH_TABLES, t * P:(t + 1) * P], picked_laid)

            def lay_group(t, g):
                lo, hi = group(t, g)
                act.wait_ge(transposed, t * NG + g + 1)
                if g == NG - 1:
                    nc.scalar.copy(denseT[:, :], bank_xt[1][:, (DENSE_SLOT - lo) * P:(DENSE_SLOT - lo + 1) * P])
                nc.scalar.copy(XT[:, :, lo:hi].rearrange("p b s -> p s b"),
                               bank_xt[1][:, 0:(hi - lo) * P].rearrange("p (s b) -> p s b", b=P)
                               ).then_inc(xt_ready[1], 1)

            def tile(t):
                more = t + 1 < TILES
                if t:
                    take_y(t - 1)
                late = EARLY + t < OH_TABLES
                if late:
                    take_picked(EARLY + t)
                elif more:
                    lay_picked_tile(t + 1)
                for q in range(Z_CHUNKS):
                    act.wait_ge(z_ready, t * Z_CHUNKS + q + 1)
                    nc.scalar.copy(zT[0:Z_ROWS, q, :], bank_zq[q][0:Z_ROWS, 0:P]).then_inc(zT_ready, 1)
                    if more and q == 1:
                        lay_group(t + 1, 1)
                if late:
                    lay_picked_tile(t + 1)
                act.wait_ge(h1_sum, t * 2 + 1)
                for m in range(M1 // 2):
                    nc.scalar.activation(h1T[:, m, :], bank_h1[0][:, m * P:(m + 1) * P], ACT.Relu,
                                         bias=b1_sb[:, m:m + 1]).then_inc(h1_act, 1)
                if more:
                    lay_group(t + 1, 3)
                    lay_group(t + 1, 5)
                act.wait_ge(h2_sum, t * 2 + 1)
                nc.scalar.activation(h2T[:, 0, :], bank_z[:, 0:P], ACT.Relu, bias=b2_sb[:, 0:1]).then_inc(h2_act, 1)
                if EARLY + t + 1 < OH_TABLES:
                    spread_ids(EARLY + t + 1)
                    take_hi(EARLY + t + 1)
                    compare(EARLY + t + 1)

            def take_y(t):
                act.wait_ge(y_sum, t + 1)
                nc.scalar.copy(y_row[:, t * P:(t + 1) * P], bank_z[0:1, 2 * P:3 * P]).then_inc(y_ready, 1)

            act.dma_start(ids_bc[0:VP, 0, :], ids_t[PICKED[0]:PICKED[0] + 1, :].to_broadcast((VP, BATCH))
                          ).then_inc(ids_bc_loaded[0], 16)
            act.wait_ge(consts_ready, 1)
            nc.scalar.mul(neg_row_id[:, :], row_id[:, :], -1.0).then_inc(neg_ready, 1)
            act.wait_ge(neg_ready, 1)
            act.wait_ge(pad_zeroed, 1)
            spread_ids(0)
            after = {3: 1, 4: 3, 6: 5}
            for k in range(EARLY):
                spread_ids(k + 1)
                take_hi(k)
                compare(k)
                if k:
                    take_picked(k - 1)
                if k in after:
                    lay_group(0, after[k])
            last = EARLY - 1
            act.wait_ge(picked_out, last)
            lay_picked(0, (oh_index(0), oh_index(last)), pickedT[:, oh_index(0):oh_index(last), 0:P], picked_laid_0)
            take_hi(EARLY)
            act.wait_ge(picked, EARLY)
            lay_picked(0, (oh_index(last), oh_index(last) + 1),
                       bank_h1[last % 2][:, 0:P].rearrange("p (s b) -> p s b", s=1), picked_laid)
            take_picked(last)
            compare(EARLY)
            act.wait_ge(weights_loaded, 16 * 5)
            for t in range(TILES):
                tile(t)
            take_y(TILES - 1)


def pair_rows():
    picked = sorted(range(OH_TABLES), key=oh_index)
    feature = [1 + f for f in GATHERED] + [0] + [1 + PICKED[k] for k in picked]
    order = []
    for j in range(SLOTS):
        for step in range(1, HALF + 1):
            a, b = sorted((feature[j], feature[(j + step) % SLOTS]))
            order.append(D + a * (2 * SLOTS - a - 1) // 2 + (b - a - 1))
    return order


def kernel(**inputs):
    import numpy as np
    import concourse.bacc as bacc
    from concourse import mybir as mb
    from concourse.bass_utils import run_bass_kernel_spmd

    ids = np.asarray(inputs["ids"])
    w1 = np.asarray(inputs["W_top1"])
    n_pairs = SLOTS * HALF
    laid = {
        "dense": np.asarray(inputs["r_dense_features"]),
        "ids_p": ids.reshape(TILES, P, NF).transpose(1, 0, 2),
        "ids_t": ids.transpose(),
        "w1_pairs": w1[np.array(pair_rows())],
        "w1_dense": np.concatenate([w1[0:D], w1[D + n_pairs:]]),
        "b1": np.asarray(inputs["b_top1"]).reshape(M1, P).transpose(),
        "w2": np.asarray(inputs["W_top2"]),
        "b2": np.asarray(inputs["b_top2"]).reshape(M2, P).transpose(),
        "w3": np.asarray(inputs["W_top3"]).reshape(M2, P).transpose(),
    }
    for f in range(NF):
        laid[f"tbl_{f}"] = np.asarray(inputs[f"tbl_{f}"])

    nc = bacc.Bacc("TRN2", target_bir_lowering=False, num_devices=1)
    arrays, args = {}, {}
    for name, a in laid.items():
        a = np.ascontiguousarray(a)
        arrays[f"in_{name}"] = a
        args[name] = nc.dram_tensor(f"in_{name}", a.shape, mb.dt.from_np(a.dtype), kind="ExternalInput").ap()
    out = nc.dram_tensor("out_y", (BATCH, 1), mb.dt.float32, kind="ExternalOutput").ap()
    tables = [args.pop(f"tbl_{f}") for f in range(NF)]
    dlrm_tower(nc, tables=tables, out=out, **args)
    result = run_bass_kernel_spmd(nc, [arrays], core_ids=[0])
    return result.results[0]["out_y"]
```
